# Optimizing a Trainium2 kernel written in Bass

```python
import numpy as np
import jax
import jax.numpy as jnp

def _softmax(x, axis=-1):
    return jax.nn.softmax(x, axis=axis)

def _gelu(x):
    return jax.nn.gelu(x, approximate=True)

def _silu(x):
    return jax.nn.silu(x)

def _sigmoid(x):
    return jax.nn.sigmoid(x)

def _layernorm(x, axis=-1, eps=1e-05):
    m = jnp.mean(x, axis=axis, keepdims=True)
    v = jnp.var(x, axis=axis, keepdims=True)
    return (x - m) / jnp.sqrt(v + eps)

def _scatter_add(tgt, idx, src, axis=0):
    return tgt.at[idx].add(src)

def _segment_sum(src, seg, n):
    return jax.ops.segment_sum(src, seg, n)
kernel_name = 'mk_rec_standalone_d1_rec_r8_9c35a6'

def setup_inputs(seed: int=0):
    np.random.seed(seed)
    _w = jnp.asarray

    def _rec_inputs():
        import jax
        import jax.numpy as jnp
        _rk = jax.random.key(seed)
        r_goods = -6.35064e-05 + 0.99983 * jax.random.normal(jax.random.fold_in(_rk, 1), (2048, 200, 32), jnp.float32)
        r_candidate_ad = -0.00499425 + 1.0058 * jax.random.normal(jax.random.fold_in(_rk, 2), (2048, 32), jnp.float32)
        return (r_goods, r_candidate_ad)
    r_goods, r_candidate_ad = _rec_inputs()

    def _L0_rec_setup():
        import jax, jax.numpy as jnp
        import numpy as np
        B, N, K = (1024, 200, 32)
        HID = 36
        IN_DIM = K * (K + 2)
        key = jax.random.key(seed)
        ks = jax.random.split(key, 4)
        candidate_ad = jax.random.normal(ks[0], (B, K), dtype=jnp.float32)
        goods = jax.random.normal(ks[1], (B, N, K), dtype=jnp.float32)
        W1 = jax.random.normal(ks[2], (IN_DIM, HID), dtype=jnp.float32) * (1.0 / np.sqrt(IN_DIM))
        b1 = jnp.zeros((HID,), dtype=jnp.float32)
        W2 = jax.random.normal(ks[3], (HID, 1), dtype=jnp.float32) * (1.0 / np.sqrt(HID))
        b2 = jnp.zeros((1,), dtype=jnp.float32)
        return {'candidate_ad': candidate_ad, 'goods': goods, 'W1': W1, 'b1': b1, 'W2': W2, 'b2': b2}
    _L0_rec_all = _L0_rec_setup()
    _L0_rec_in = {k: v for k, v in _L0_rec_all.items() if k in ('W1', 'b1', 'W2', 'b2')}
    del _L0_rec_all
    return {'r_goods': r_goods, 'r_candidate_ad': r_candidate_ad, 'L0_rec_W1': _L0_rec_in['W1'], 'L0_rec_b1': _L0_rec_in['b1'], 'L0_rec_W2': _L0_rec_in['W2'], 'L0_rec_b2': _L0_rec_in['b2']}

def reference(r_goods, r_candidate_ad, L0_rec_W1, L0_rec_b1, L0_rec_W2, L0_rec_b2):
    import jax
    import jax.numpy as jnp

    def _L0_rec_ref(candidate_ad, goods, W1, b1, W2, b2):
        import jax, jax.numpy as jnp
        import numpy as np
        B, N, K = (1024, 200, 32)
        HID = 36
        IN_DIM = K * (K + 2)
        Bs, Ns, Ks = goods.shape
        outer = jnp.einsum('bi,bnj->bnij', candidate_ad, goods).reshape(Bs, Ns, Ks * Ks)
        k_b = jnp.broadcast_to(candidate_ad[:, None, :], (Bs, Ns, Ks))
        h1 = jnp.concatenate((k_b, goods, outer), axis=-1)
        act = jax.nn.sigmoid(h1 @ W1 + b1)
        weight = act @ W2 + b2
        out = jnp.sum(goods * weight, axis=1)
        return out
    y = _L0_rec_ref(r_candidate_ad, r_goods, L0_rec_W1, L0_rec_b1, L0_rec_W2, L0_rec_b2)
    return y

_drawn_inputs = setup_inputs


def setup_inputs(seed=0):
    import zlib

    import numpy as np

    out = dict(_drawn_inputs(seed))
    spreads = {'L0_rec_b1': (0.0, 0.352)}
    factors = {}
    for name, (base, spread) in spreads.items():
        noise = np.random.default_rng([zlib.crc32(name.encode()), seed]).standard_normal(out[name].shape)
        drawn = base * np.exp(spread * noise) if base else spread * noise
        out[name] = jnp.asarray(drawn.astype(out[name].dtype))
    for name, factor in factors.items():
        out[name] = (out[name] * factor).astype(out[name].dtype)
    return out
```

```python
from contextlib import ExitStack

import concourse.bass as bass
from concourse import mybir

F32 = mybir.dt.float32
BF16 = mybir.dt.bfloat16
ALU = mybir.AluOpType
ACT = mybir.ActivationFunctionType

P = 128
B, N, K, H = 2048, 200, 32, 36
Q = 4
S = 4
HM = 32
HR = H - HM
TILE_B = Q * S
TILES = B // TILE_B
BLOCK = 8
PAIRS = BLOCK // 2
BLOCKS = TILES // BLOCK
GROUPS = TILES * S
UNROLL = 2 * BLOCK
TURNS = TILES // UNROLL
BD_SLOTS = 4
LAG = 12
PARTS = 3
LOAD_AHEAD = 4
STACK_AT = (1, 2, 4, 5)
W1_CHUNKS = 6
BANK = 512

C_QMASK = 0
C_B1M = C_QMASK + Q
C_B1R = C_B1M + 1
C_B2 = C_B1R + 1
C_W1B = C_B2 + 1
C_W1AM = C_W1B + H
C_W1AR = C_W1AM + P
C_W2M = C_W1AR + 2 * HM
C_W2R = C_W2M + 2 * S * 32
C_ALL = C_W2R + 32


def build(nc, goods_t, cand_t, w1_outer, small, spread, out_t):
    with ExitStack() as ctx:
        def sb(name, shape, dt=F32):
            return ctx.enter_context(nc.sbuf_tensor(name, shape, dt))

        def ps(name, shape):
            return ctx.enter_context(nc.psum_tensor(name, shape, F32))

        def sem(name):
            return ctx.enter_context(nc.semaphore(name))

        goods = sb("goods", [P, UNROLL, S, N])
        act = sb("act", [P, UNROLL, S, N])
        act_rest = sb("act_rest", [P, UNROLL // 2, N])
        wb = sb("wb", [P, H, GROUPS])
        bd_main = sb("bd_main", [P, BD_SLOTS, S, Q, HM])
        bd_rest = sb("bd_rest", [P, BD_SLOTS, S, 2, Q, HR])
        consts = sb("consts", [P, C_ALL])
        spread_sb = sb("spread_sb", [PARTS * 32, 2 * S, P], BF16)
        bias_main = sb("bias_main", [P, GROUPS])
        bias_rest = sb("bias_rest", [P, TILES // 2])
        wsum = sb("wsum", [P, N])
        left = sb("left", [P, N])
        parts = sb("parts", [P, PARTS, N], BF16)
        stack = sb("stack", [PARTS * 32, 2, PAIRS, N], BF16)
        out_stage = sb("out_stage", [P, 2, BLOCK * S])

        act_flat = act[:, :, :, :].rearrange("p u s n -> p (u s n)")
        w1_bd = act_flat[:, 0:H * P].rearrange("p (h c) -> p h c", h=H)
        cand = act_flat[:, H * P:H * P + GROUPS]

        qmask = consts[:, C_QMASK:C_QMASK + Q]
        b1_main = consts[:, C_B1M:C_B1M + 1]
        b1_rest = consts[:, C_B1R:C_B1R + 1]
        b2 = consts[:, C_B2:C_B2 + 1]
        w1_goods = consts[:, C_W1B:C_W1B + H]
        w1a_main = consts[:, C_W1AM:C_W1AM + P]
        w1a_rest = consts[:, C_W1AR:C_W1AR + 64].rearrange("p (t c) -> p t c", t=2)
        w2_main = consts[:, C_W2M:C_W2M + 2 * S * 32].rearrange("p (v c) -> p v c", v=2 * S)
        w2_rest = consts[:, C_W2R:C_W2R + 32]

        z_ps = [[ps(f"z_ps{a}{b}", [P, BANK]) for b in range(2)] for a in range(2)]
        rest_ps = ps("rest_ps", [P, BANK])
        w_ps = ps("w_ps", [P, BANK])
        spread_ps = [ps(f"spread_ps{a}", [P, BANK]) for a in range(2)]
        wb_ps = [z_ps[0][0], z_ps[0][1], z_ps[1][0], z_ps[1][1]]

        consts_loaded = sem("consts_loaded")
        cand_loaded = sem("cand_loaded")
        spread_loaded = sem("spread_loaded")
        w1_loaded = [sem(f"w1_loaded{i}") for i in range(W1_CHUNKS)]
        goods_loaded = [sem(f"goods_loaded{i}") for i in range(UNROLL)]
        stack_loaded = [sem(f"stack_loaded{m}") for m in range(PAIRS)]
        out_stored = sem("out_stored")
        wb_made = sem("wb_made")
        wb_kept_dve = sem("wb_kept_dve")
        wb_kept_act = sem("wb_kept_act")
        bias_made = sem("bias_made")
        bias_kept = sem("bias_kept")
        bd_zeroed = sem("bd_zeroed")
        bd_ready = sem("bd_ready")
        z_done = sem("z_done")
        rest_done = sem("rest_done")
        act_done = sem("act_done")
        act_rest_done = sem("act_rest_done")
        w_done = sem("w_done")
        w_read = sem("w_read")
        part_step = sem("part_step")
        spread_done = sem("spread_done")
        pooled = sem("pooled")

        block = ctx.enter_context(nc.Block())

        def turns(eng, step):
            for u in range(UNROLL):
                step(0, u)
            with eng.Fori(1, TURNS) as turn:
                for u in range(UNROLL):
                    step(turn, u)

        def reached(turn, u, least):
            return not isinstance(turn, int) or UNROLL * turn + u >= least


        @block.sync
        def _(sp):
            sp.dma_start(cand, cand_t[:, :]).then_inc(cand_loaded, 16)
            step_h = H // W1_CHUNKS
            for c in range(W1_CHUNKS):
                sp.dma_start(w1_bd[:, c * step_h:(c + 1) * step_h, :],
                             w1_outer[:, c * step_h:(c + 1) * step_h, :]).then_inc(w1_loaded[c], 16)

            def stack_pair(turn, v, m):
                k = 2 * turn + v // BLOCK
                sp.wait_ge(part_step, 4 * k + 4)
                for part in range(PARTS):
                    sp.dma_start(stack[32 * part:32 * part + 32, (v // BLOCK) % 2, m, :],
                                 parts[32 * m:32 * m + 32, part, :]).then_inc(stack_loaded[m], 16)

            def stack_step(turn, u):
                for m, at in enumerate(STACK_AT):
                    first = u - LOAD_AHEAD - BLOCK - at
                    if first % BLOCK == 0 and first > -2 * UNROLL and reached(turn, u, LOAD_AHEAD + BLOCK + at):
                        if not isinstance(turn, int) or first + UNROLL * turn < TILES:
                            stack_pair(turn, first, m)

            def store(turn, v):
                k = 2 * turn + v // BLOCK
                sp.wait_ge(pooled, 2 * BLOCK * k + 2 * BLOCK)
                sp.dma_start(out_t[:, bass.ds(BLOCK * S * k, BLOCK * S)],
                             out_stage[:, (v // BLOCK) % 2, :]).then_inc(out_stored, 16)

            def step(turn, u):
                stack_step(turn, u)
                if u == BLOCK and reached(turn, u, UNROLL):
                    store(turn, -UNROLL)
                if u == UNROLL - 1 and reached(turn, u, UNROLL):
                    store(turn, -BLOCK)
                if reached(turn, u, UNROLL):
                    sp.wait_ge(pooled, 2 * (UNROLL * turn + u - UNROLL) + 2)
                sp.dma_start(goods[:, u, :, :].rearrange("p s n -> p (s n)"),
                             goods_t[:, bass.ds(UNROLL * turn + u, 1), :].rearrange("p o n -> p (o n)")
                             ).then_inc(goods_loaded[u], 16)

            turns(sp, step)
            for u in range(LOAD_AHEAD + max(STACK_AT) + 1):
                stack_step(TURNS, u)
            store(TURNS, -16)
            store(TURNS, -8)
            sp.wait_ge(out_stored, 16 * BLOCKS)

        @block.gpsimd
        def _(pool):
            nc.gpsimd.memset(bd_rest[:, :, :, :, :, :].rearrange("p a s t q h -> p (a s t q h)"), 0.0).then_inc(bd_zeroed, 1)
            pool.wait_ge(bd_zeroed, 1)
            pool.wait_ge(consts_loaded, 16)
            pool.wait_ge(wb_kept_dve, H // 2)
            pool.wait_ge(wb_kept_act, H // 2)

            def step(turn, u):
                slot = u % BD_SLOTS
                if reached(turn, u, BD_SLOTS):
                    pool.wait_ge(rest_done, UNROLL * turn + u - BD_SLOTS + 1)
                for lo, n, dst in ((0, HM, bd_main[:, slot, :, :, :]),
                                   (HM, HR, bd_rest[:, slot, :, u % 2, :, :])):
                    src = wb[:, lo:lo + n, bass.ds(S * (UNROLL * turn + u), S)].rearrange("p h s -> p s h")
                    nc.gpsimd.tensor_tensor(
                        dst, src.unsqueeze(2).broadcast_to([P, S, Q, n]),
                        qmask.unsqueeze(1).unsqueeze(3).broadcast_to([P, S, Q, n]), ALU.mult).then_inc(bd_ready, 1)

            turns(pool, step)

        @block.tensor
        def _(pe):
            pe.wait_ge(cand_loaded, 16)
            for h in range(H):
                if h % (H // W1_CHUNKS) == 0:
                    pe.wait_ge(w1_loaded[h // (H // W1_CHUNKS)], 16)
                if h >= 4:
                    pe.wait_ge(wb_kept_act if h % 2 else wb_kept_dve, h // 2 - 1)
                nc.tensor.matmul(wb_ps[h % 4][:, :], w1_bd[:, h, :], cand,
                                 start=True, stop=True).then_inc(wb_made, 1)
            pe.wait_ge(consts_loaded, 16)
            nc.tensor.matmul(w_ps[:, :], w1a_main, cand, start=True, stop=True)
            cand_v = cand.rearrange("p (m t s) -> p m t s", t=2, s=S)
            for s in range(S):
                for t in range(2):
                    last = nc.tensor.matmul(rest_ps[32 * s:32 * s + 32, 0:TILES // 2], w1a_rest[:, t, :],
                                            cand_v[:, :, t, s], start=(t == 0), stop=(t == 1))
            last.then_inc(bias_made, 1)
            pe.wait_ge(spread_loaded, 16)
            pe.wait_ge(bias_kept, 2)

            def row_sums(turn, u):
                v = u - BLOCK
                k = 2 * turn + v // BLOCK
                s0 = UNROLL * turn + u
                pe.wait_ge(act_done, 2 * s0)
                pe.wait_ge(act_rest_done, BLOCK // 2 * (k + 1))
                if not isinstance(k, int) or k >= 1:
                    pe.wait_ge(w_read, k)
                for t in range(2):
                    for s in range(S):
                        for m in range(PAIRS):
                            nc.tensor.matmul(w_ps[32 * m:32 * m + 32, 0:N], w2_main[:, S * t + s, :],
                                             act[:, (v + 2 * m + t) % UNROLL, s, :],
                                             start=(t == 0 and s == 0), stop=False)
                for m in range(PAIRS):
                    last = nc.tensor.matmul(w_ps[32 * m:32 * m + 32, 0:N], w2_rest,
                                            act_rest[:, ((v + 2 * m) % UNROLL) // 2, :], start=False, stop=True)
                last.then_inc(w_done, 1)

            def spread_step(turn, v):
                t8 = v % BLOCK
                k = 2 * turn + v // BLOCK
                tile = UNROLL * turn + v
                if t8 % 2 == 0:
                    pe.wait_ge(stack_loaded[t8 // 2], 16 * PARTS * (k + 1))
                for half in range(2):
                    if not isinstance(tile, int) or tile >= 1:
                        pe.wait_ge(pooled, 2 * (tile - 1) + half + 1)
                    for s in range(2 * half, 2 * half + 2):
                        last = nc.tensor.matmul(spread_ps[half][:, N * (s % 2):N * (s % 2) + N],
                                                spread_sb[:, S * (t8 % 2) + s, :],
                                                stack[:, (v // BLOCK) % 2, t8 // 2, :], start=True, stop=True)
                    last.then_inc(spread_done, 1)

            def step(turn, u):
                tile = UNROLL * turn + u
                slot = u % BD_SLOTS
                pe.wait_ge(goods_loaded[u], 16 * (turn + 1))
                pe.wait_ge(bd_ready, 2 * tile + 2)
                for half in range(2):
                    if reached(turn, u, 2):
                        pe.wait_ge(act_done, 2 * (tile - 2) + half + 1)
                    for s in range(2 * half, 2 * half + 2):
                        last = nc.tensor.matmul(z_ps[u % 2][half][:, N * (s % 2):N * (s % 2) + N],
                                                bd_main[:, slot, s, :, :].rearrange("p q h -> p (q h)"),
                                                goods[:, u, s, :], start=True, stop=True)
                    last.then_inc(z_done, 1)
                if u % 2 == 0 and reached(turn, u, 2):
                    pe.wait_ge(act_rest_done, UNROLL // 2 * turn + u // 2)
                for s in range(S):
                    last = nc.tensor.matmul(rest_ps[32 * s:32 * s + 32, 0:N],
                                            bd_rest[:, slot, s, :, :, :].rearrange("p t q h -> p (t q h)"),
                                            goods[:, u, s, :], start=(u % 2 == 0), stop=(u % 2 == 1))
                last.then_inc(rest_done, 1)
                if reached(turn, u, LAG):
                    spread_step(turn, u - LAG)
                if u % BLOCK == 0 and reached(turn, u, BLOCK):
                    row_sums(turn, u)

            turns(pe, step)
            row_sums(TURNS, 0)
            for u in range(LAG):
                spread_step(TURNS, u - LAG)

        @block.scalar
        def _(sc):
            sc.dma_start(consts[:, :], small[:, :]).then_inc(consts_loaded, 16)
            sc.dma_start(spread_sb[:, :, :], spread[:, :, :]).then_inc(spread_loaded, 16)
            sc.wait_ge(consts_loaded, 16)
            for h in range(1, H, 2):
                sc.wait_ge(wb_made, h + 1)
                nc.scalar.activation(wb[:, h, :], wb_ps[h % 4][:, :], ACT.Identity,
                                     bias=w1_goods[:, h:h + 1]).then_inc(wb_kept_act, 1)
            sc.wait_ge(bias_kept, 2)

            def step(turn, u):
                tile = UNROLL * turn + u
                if u % BLOCK == 0 and reached(turn, u, UNROLL):
                    sc.wait_ge(w_done, 2 * turn + u // BLOCK - 1)
                for half in range(2):
                    sc.wait_ge(z_done, 2 * tile + half + 1)
                    for s in range(2 * half, 2 * half + 2):
                        last = nc.scalar.activation(act[:, u, s, :],
                                                    z_ps[u % 2][half][:, N * (s % 2):N * (s % 2) + N], ACT.Sigmoid,
                                                    bias=bias_main[:, bass.ds(S * tile + s, 1)])
                    last.then_inc(act_done, 1)
                if u % 2 == 1:
                    sc.wait_ge(rest_done, tile + 1)
                    nc.scalar.activation(act_rest[:, u // 2, :], rest_ps[:, 0:N], ACT.Sigmoid,
                                         bias=bias_rest[:, bass.ds(UNROLL // 2 * turn + u // 2, 1)]
                                         ).then_inc(act_rest_done, 1)

            turns(sc, step)

        @block.vector
        def _(dve):
            dve.wait_ge(consts_loaded, 16)
            for h in range(0, H, 2):
                dve.wait_ge(wb_made, h + 1)
                nc.vector.tensor_scalar(wb[:, h, :], wb_ps[h % 4][:, :], w1_goods[:, h:h + 1], None,
                                        ALU.add).then_inc(wb_kept_dve, 1)
            dve.wait_ge(bias_made, 1)
            nc.vector.tensor_scalar(bias_main[:, :], w_ps[:, :], b1_main, None, ALU.add).then_inc(bias_kept, 1)
            nc.vector.tensor_scalar(bias_rest[:, :], rest_ps[:, 0:TILES // 2], b1_rest, None,
                                    ALU.add).then_inc(bias_kept, 1)

            def cut(turn, u):
                k = 2 * turn + (u - BLOCK) // BLOCK
                dve.wait_ge(w_done, k + 1)
                nc.vector.tensor_scalar(wsum[:, :], w_ps[:, 0:N], b2, None, ALU.add).then_inc(w_read, 1)
                if not isinstance(k, int) or k >= 1:
                    for m in range(PAIRS):
                        dve.wait_ge(stack_loaded[m], 16 * PARTS * k)
                dve.wait_ge(w_read, k + 1)
                nc.vector.tensor_copy(parts[:, 0, :], wsum[:, :]).then_inc(part_step, 1)
                dve.wait_ge(part_step, 4 * k + 1)
                nc.vector.tensor_tensor(left[:, :], wsum[:, :], parts[:, 0, :], ALU.subtract).then_inc(part_step, 1)
                dve.wait_ge(part_step, 4 * k + 2)
                nc.vector.tensor_copy(parts[:, 1, :], left[:, :]).then_inc(part_step, 1)
                dve.wait_ge(part_step, 4 * k + 3)
                nc.vector.tensor_tensor(parts[:, 2, :], left[:, :], parts[:, 1, :],
                                        ALU.subtract).then_inc(part_step, 1)

            def pool_step(turn, v):
                t8 = v % BLOCK
                k = 2 * turn + v // BLOCK
                tile = UNROLL * turn + v
                if t8 == 0 and (not isinstance(k, int) or k >= 2):
                    dve.wait_ge(out_stored, 16 * (k - 1))
                for half in range(2):
                    dve.wait_ge(spread_done, 2 * tile + half + 1)
                    for s in range(2 * half, 2 * half + 2):
                        last = nc.vector.tensor_tensor_reduce(
                            goods[:, v % UNROLL, s, :], spread_ps[half][:, N * (s % 2):N * (s % 2) + N],
                            goods[:, v % UNROLL, s, :], 1.0, 0.0, ALU.mult, ALU.add,
                            out_stage[:, (v // BLOCK) % 2, S * t8 + s:S * t8 + s + 1])
                    last.then_inc(pooled, 1)

            def step(turn, u):
                if reached(turn, u, LAG):
                    pool_step(turn, u - LAG)
                if u % BLOCK == 0 and reached(turn, u, BLOCK):
                    cut(turn, u)

            turns(dve, step)
            cut(TURNS, 0)
            for u in range(LAG):
                pool_step(TURNS, u - LAG)


def kernel(r_goods, r_candidate_ad, L0_rec_W1, L0_rec_b1, L0_rec_W2, L0_rec_b2):
    import numpy as np
    import concourse.bacc as bacc
    from concourse.bass_utils import run_bass_kernel_spmd

    f32 = np.float32
    w1 = np.asarray(L0_rec_W1)
    b1 = np.asarray(L0_rec_b1)
    w2 = np.asarray(L0_rec_W2)[:, 0]
    w1_cand, w1_goods, w1_out = w1[:K], w1[K:2 * K], w1[2 * K:].reshape(K, K, H)

    goods_t = np.ascontiguousarray(
        np.asarray(r_goods).reshape(TILES, Q, S, N, K).transpose(1, 4, 0, 2, 3)).reshape(P, TILES, S * N)
    cand_t = np.ascontiguousarray(
        np.asarray(r_candidate_ad).reshape(TILES, Q, S, K).transpose(1, 3, 0, 2)).reshape(P, GROUPS)

    w1_outer = np.zeros((Q, K, H, Q, K), f32)
    w1a_main = np.zeros((Q, K, Q, HM), f32)
    w1a_rest = np.zeros((Q, K, 2, 2, Q, HR), f32)
    w2_main = np.zeros((Q, HM, 2, S, 2, S, Q), f32)
    w2_rest = np.zeros((S, 2, Q, HR, 2, S, Q), f32)
    qmask = np.zeros((Q, K, Q), f32)
    for q in range(Q):
        w1_outer[q, :, :, q, :] = w1_out.transpose(0, 2, 1)
        w1a_main[q, :, q, :] = w1_cand[:, :HM]
        qmask[q, :, q] = 1.0
        for t in range(2):
            w1a_rest[q, :, t, t, q, :] = w1_cand[:, HM:]
            for s in range(S):
                w2_main[q, :, t, s, t, s, q] = w2[:HM]
                w2_rest[s, t, q, :, t, s, q] = w2[HM:]
    small = np.zeros((P, C_ALL), f32)
    small[:, C_QMASK:C_B1M] = qmask.reshape(P, Q)
    small[:, C_B1M] = np.tile(b1[:HM], Q)
    small[:, C_B1R] = np.tile(b1[HM:], S * 2 * Q)
    small[:, C_B2] = np.asarray(L0_rec_b2)[0]
    small[:, C_W1B:C_W1AM] = np.tile(w1_goods, (Q, 1))
    small[:, C_W1AM:C_W1AR] = w1a_main.reshape(P, P)
    small[:, C_W1AR:C_W2M] = w1a_rest.reshape(P, 64)
    small[:, C_W2M:C_W2R] = w2_main.reshape(P, 2 * S * 32)
    small[:, C_W2R:C_ALL] = w2_rest.reshape(P, 32)

    bf16 = mybir.dt.np(BF16)
    spread = np.zeros((PARTS, 2, S, Q, 2, S, Q, K), bf16)
    for t in range(2):
        for s in range(S):
            for q in range(Q):
                spread[:, t, s, q, t, s, q, :] = 1.0
    spread = spread.reshape(PARTS * 32, 2 * S, P)

    nc = bacc.Bacc("TRN2", target_bir_lowering=False, num_devices=1)
    arrays, args = {}, []
    for name, a in (("goods_t", goods_t), ("cand_t", cand_t), ("w1_outer", w1_outer.reshape(P, H, P)),
                    ("small", small), ("spread", spread)):
        arrays[name] = a
        args.append(nc.dram_tensor(name, a.shape, mybir.dt.from_np(a.dtype), kind="ExternalInput").ap())
    out_t = nc.dram_tensor("out_t", (P, GROUPS), F32, kind="ExternalOutput").ap()
    build(nc, *args, out_t)
    r = run_bass_kernel_spmd(nc, [arrays], core_ids=[0])
    got = np.asarray(r.results[0]["out_t"]).reshape(Q, K, TILES, S)
    return np.ascontiguousarray(got.transpose(2, 0, 3, 1)).reshape(B, K)
```

```python
from contextlib import ExitStack

import concourse.bass as bass
from concourse import mybir

F32 = mybir.dt.float32
BF16 = mybir.dt.bfloat16
ALU = mybir.AluOpType
ACT = mybir.ActivationFunctionType

P = 128
B, N, K, H = 2048, 200, 32, 36
Q = 4
HALF_H = H // 2
ROWS = 3 * H + HALF_H
DUO_B = 7
U = 4
DUOS = 294
UNITS = 2 * DUOS
TILES = UNITS // U
BLOCK = 4
COL_TILES = 4
DUOS_C = BLOCK * U // 2 // COL_TILES
SLOTS = 16
TURNS = TILES // SLOTS
REST = TILES - TURNS * SLOTS
TURN_BLOCKS = SLOTS // BLOCK
BLOCKS = TURNS * TURN_BLOCKS
ACT_SLOTS = 8
BD_SLOTS = 4
SUM_LAG = 2
LAG = 10
PARTS = 3
CUT_AT = BLOCK + 2
MOVE_AT = 12
WIDE = 1
WIDE_SLOTS = 2 * BLOCK
WIDEN_AT = (0, 1, 2, 3)
LOAD = 1
STORE = 8
W1_CHUNKS = 6
BANK = 512

C_QMASK = 0
C_B1 = C_QMASK + Q
C_B2 = C_B1 + 2
C_W1B = C_B2 + 1
C_W1A = C_W1B + H
C_W2 = C_W1A + 2 * P
C_ALL = C_W2 + DUOS_C * 2 * 32


def build(nc, goods_t, cand_t, w1_outer, small, spread, out_t):
    with ExitStack() as ctx:
        def sb(name, shape, dt=F32):
            return ctx.enter_context(nc.sbuf_tensor(name, shape, dt))

        def ps(name, shape):
            return ctx.enter_context(nc.psum_tensor(name, shape, F32))

        def sem(name):
            return ctx.enter_context(nc.semaphore(name))

        goods = sb("goods", [P, SLOTS, U, N])
        act = sb("act", [P, ACT_SLOTS, U, N])
        wb = sb("wb", [P, H, DUOS, 2])
        bd = sb("bd", [P, BD_SLOTS, U, ROWS])
        consts = sb("consts", [P, C_ALL])
        spread_sb = sb("spread_sb", [PARTS * 32, DUOS_C * 2, P], BF16)
        bias = sb("bias", [P, DUOS, 2])
        wsum = sb("wsum", [P, 2, N])
        wide = sb("wide", [P, WIDE_SLOTS, WIDE, N])
        left = sb("left", [P, N])
        parts = sb("parts", [P, PARTS, N], BF16)
        stack = sb("stack", [PARTS * 32, 2, COL_TILES, N], BF16)
        out_stage = sb("out_stage", [P, SLOTS * U])

        act_flat = act[:, :, :, :].rearrange("p t u n -> p (t u n)")
        w1_bd = act_flat[:, 0:H * P].rearrange("p (h c) -> p h c", h=H)
        cand = act_flat[:, H * P:H * P + UNITS].rearrange("p (a d) -> p a d", a=2)

        qmask = consts[:, C_QMASK:C_QMASK + Q]
        b1 = consts[:, C_B1:C_B1 + 2]
        b2 = consts[:, C_B2:C_B2 + 1]
        w1_goods = consts[:, C_W1B:C_W1B + H]
        w1_cand = consts[:, C_W1A:C_W1A + 2 * P].rearrange("p (a c) -> p a c", a=2)
        w2 = consts[:, C_W2:C_ALL].rearrange("p (v c) -> p v c", c=32)
        bias_flat = bias[:, :, :].rearrange("p d a -> p (d a)")

        z_ps = [[ps(f"z_ps{a}{b}", [P, BANK]) for b in range(2)] for a in range(2)]
        w_ps = [ps(f"w_ps{a}", [P, BANK]) for a in range(2)]
        spread_ps = [ps(f"spread_ps{a}", [P, BANK]) for a in range(2)]
        wb_ps = [z_ps[0][0], z_ps[0][1], z_ps[1][0], z_ps[1][1]]

        consts_loaded = sem("consts_loaded")
        cand_loaded = sem("cand_loaded")
        spread_loaded = sem("spread_loaded")
        w1_loaded = [sem(f"w1_loaded{i}") for i in range(W1_CHUNKS)]
        goods_loaded = [sem(f"goods_loaded{i}") for i in range(SLOTS // LOAD)]
        stack_loaded = [sem(f"stack_loaded{m}") for m in range(COL_TILES)]
        wide_loaded = [sem(f"wide_loaded{i}") for i in range(WIDE_SLOTS)]
        out_stored = [sem(f"out_stored{i}") for i in range(SLOTS // STORE)]
        wb_made = sem("wb_made")
        wb_kept = [sem("wb_kept0"), sem("wb_kept1")]
        bias_made = sem("bias_made")
        bias_kept = sem("bias_kept")
        bd_ready = sem("bd_ready")
        z_done = sem("z_done")
        act_done = sem("act_done")
        w_made = sem("w_made")
        w_kept = sem("w_kept")
        part_step = sem("part_step")
        spread_done = sem("spread_done")
        pooled = sem("pooled")

        block = ctx.enter_context(nc.Block())

        def turns(eng, step):
            for u in range(SLOTS):
                step(0, u)
            with eng.Fori(1, TURNS) as turn:
                for u in range(SLOTS):
                    step(turn, u)

        def reached(turn, u, least):
            return not isinstance(turn, int) or SLOTS * turn + u >= least

        @block.sync
        def _(sp):
            sp.dma_start(cand, cand_t[:, :, :]).then_inc(cand_loaded, 16)
            step_h = H // W1_CHUNKS
            for c in range(W1_CHUNKS):
                sp.dma_start(w1_bd[:, c * step_h:(c + 1) * step_h, :],
                             w1_outer[:, c * step_h:(c + 1) * step_h, :]).then_inc(w1_loaded[c], 16)

            def move(k, half):
                sp.wait_ge(part_step, 3 * k + 3)
                for m in range(COL_TILES):
                    sp.dma_start(stack[:, half, m, :], parts[32 * m:32 * m + 32, :, :]).then_inc(stack_loaded[m], 16)

            def widen(half, v):
                for w in range(WIDE):
                    row = 32 * (v % 2 * 2 + w) + DUO_B * (v // 2)
                    sp.dma_start(wide[:, BLOCK * half + v, w, :],
                                 wsum[row:row + Q, half, :].unsqueeze(1).broadcast_to([Q, K, N])
                                 ).then_inc(wide_loaded[BLOCK * half + v], 16)

            def moves(turn, u):
                first = (u - MOVE_AT) // BLOCK * BLOCK
                if reached(turn, u, MOVE_AT):
                    if u - MOVE_AT == first:
                        move(TURN_BLOCKS * turn + first // BLOCK, (first // BLOCK) % 2)
                    for v in range(BLOCK):
                        if WIDEN_AT[v] == (u - MOVE_AT - first) and (turn is not TURNS or first + v < REST):
                            widen((first // BLOCK) % 2, v)

            def store(turn, offset, tiles):
                tile = SLOTS * turn + offset
                sp.wait_ge(pooled, 2 * (tile + tiles))
                sp.dma_start(out_t[:, bass.ds(U * tile, U * tiles)],
                             out_stage[:, U * offset:U * (offset + tiles)]).then_inc(out_stored[offset // STORE], 16)

            def step(turn, u):
                moves(turn, u)
                if u % STORE == STORE - 1 and reached(turn, u, SLOTS):
                    store(turn - 1, u + 1 - STORE, STORE)
                if u % LOAD == 0:
                    load(turn, u, LOAD)

            def load(turn, u, tiles):
                tile = SLOTS * turn + u
                if reached(turn, u, SLOTS):
                    sp.wait_ge(pooled, 2 * (tile - SLOTS + tiles))
                sp.dma_start(goods[:, u:u + tiles, :, :].rearrange("p t s n -> p (t s n)"),
                             goods_t[:, bass.ds(tile, tiles), :].rearrange("p t n -> p (t n)")
                             ).then_inc(goods_loaded[u // LOAD], 16)

            turns(sp, step)
            for u in range(MOVE_AT + REST):
                if u < REST and u % LOAD == 0:
                    load(TURNS, u, min(LOAD, REST - u))
                moves(TURNS, u)
            store(TURNS - 1, 0, STORE)
            store(TURNS - 1, STORE, STORE)
            store(TURNS, 0, REST)
            sp.wait_ge(out_stored[0], 16 * (TURNS + 1))
            sp.wait_ge(out_stored[1], 16 * TURNS)

        @block.gpsimd
        def _(pool):
            pool.wait_ge(consts_loaded, 16)
            pool.wait_ge(wb_kept[0], H)
            pool.wait_ge(wb_kept[1], H)

            def step(turn, u):
                slot = u % BD_SLOTS
                tile = SLOTS * turn + u
                if reached(turn, u, BD_SLOTS):
                    pool.wait_ge(z_done, 2 * (tile - BD_SLOTS) + 2)
                src = wb[:, :, bass.ds(U // 2 * tile, U // 2), :].rearrange("p h d a -> p (d a) h")
                nc.gpsimd.tensor_tensor(
                    bd[:, slot, :, 0:3 * H].rearrange("p u (q h) -> p u q h", q=3),
                    src.unsqueeze(2).broadcast_to([P, U, 3, H]),
                    qmask[:, 0:3].unsqueeze(1).unsqueeze(3).broadcast_to([P, U, 3, H]), ALU.mult).then_inc(bd_ready, 1)
                for a in range(2):
                    src = wb[:, HALF_H * a:HALF_H * (a + 1), bass.ds(U // 2 * tile, U // 2), a]
                    nc.gpsimd.tensor_tensor(
                        bd[:, slot, a::2, 3 * H:ROWS], src.rearrange("p h d -> p d h"),
                        qmask[:, 3:4].unsqueeze(1).broadcast_to([P, U // 2, HALF_H]), ALU.mult).then_inc(bd_ready, 1)

            turns(pool, step)
            for u in range(REST):
                step(TURNS, u)

        @block.tensor
        def _(pe):
            pe.wait_ge(cand_loaded, 16)
            for h in range(H):
                if h % (H // W1_CHUNKS) == 0:
                    pe.wait_ge(w1_loaded[h // (H // W1_CHUNKS)], 16)
                for a in range(2):
                    if h >= 2:
                        pe.wait_ge(wb_kept[a], h - 1)
                    nc.tensor.matmul(wb_ps[2 * (h % 2) + a][:, 0:DUOS], w1_bd[:, h, :], cand[:, a, :],
                                     start=True, stop=True).then_inc(wb_made, 1)
            pe.wait_ge(consts_loaded, 16)
            for a in range(2):
                nc.tensor.matmul(spread_ps[a][:, 0:DUOS], w1_cand[:, a, :], cand[:, a, :],
                                 start=True, stop=True).then_inc(bias_made, 1)
            pe.wait_ge(spread_loaded, 16)
            pe.wait_ge(bias_kept, 2)

            def row_sums(turn, v, a, tiles=2):
                tile = SLOTS * turn + v
                k = TURN_BLOCKS * turn + v // BLOCK
                if a == 0:
                    pe.wait_ge(act_done, 2 * (tile + tiles))
                    if v % BLOCK == 0 and (not isinstance(k, int) or k >= 2):
                        pe.wait_ge(w_kept, 2 * (k - 1))
                d = v % BLOCK // 2
                short = isinstance(tile, int) and tile + 2 > TILES
                for m in range(U // 2 * tiles):
                    last = nc.tensor.matmul(w_ps[v // BLOCK % 2][32 * m:32 * m + 32, 0:N], w2[0:ROWS, 2 * d + a, :],
                                            act[0:ROWS, (v + m // 2) % ACT_SLOTS, m % 2 * 2 + a, :],
                                            start=(d == 0 and a == 0),
                                            stop=(a == 1 and (d == DUOS_C - 1 or isinstance(tile, int)
                                                              and tile + 2 * tiles > TILES)),
                                            skip_group_check=True)
                last.then_inc(w_made, 1)

            def spread_half(turn, v, half):
                k = TURN_BLOCKS * turn + v // BLOCK
                tile = SLOTS * turn + v
                m, d = v % 2 * 2 + half, v % BLOCK // 2
                if v % BLOCK < 2:
                    pe.wait_ge(stack_loaded[m], 16 * (k + 1))
                if not isinstance(tile, int) or tile >= 1:
                    pe.wait_ge(pooled, 2 * (tile - 1) + half + 1)
                for a in range(1 if half < WIDE else 0, 2):
                    last = nc.tensor.matmul(spread_ps[half][:, N * a:N * a + N], spread_sb[:, 2 * d + a, :],
                                            stack[:, (v // BLOCK) % 2, m, :], start=True, stop=True)
                last.then_inc(spread_done, 1)

            def products(turn, u, half):
                tile = SLOTS * turn + u
                if half == 0:
                    if u % LOAD == 0:
                        pe.wait_ge(goods_loaded[u // LOAD], 16 * (turn + 1))
                    pe.wait_ge(bd_ready, 3 * tile + 3)
                if reached(turn, u, 2):
                    pe.wait_ge(act_done, 2 * (tile - 2) + half + 1)
                for a in range(2):
                    last = nc.tensor.matmul(z_ps[u % 2][half][0:ROWS, N * a:N * a + N],
                                            bd[:, u % BD_SLOTS, 2 * half + a, :], goods[:, u, 2 * half + a, :],
                                            start=True, stop=True)
                last.then_inc(z_done, 1)

            def step(turn, u):
                for half in range(2):
                    if reached(turn, u, LAG):
                        spread_half(turn, u - LAG, half)
                    products(turn, u, half)
                if reached(turn, u, SUM_LAG):
                    row_sums(turn, u - 2 - u % 2, u % 2)

            turns(pe, step)
            for u in range(REST):
                step(TURNS, u)
            row_sums(TURNS, 0, 1)
            for a in range(2):
                row_sums(TURNS, 2, a, tiles=1)
            for u in range(REST, LAG + REST):
                for half in range(2):
                    spread_half(TURNS, u - LAG, half)

        @block.scalar
        def _(sc):
            sc.dma_start(consts[:, :], small[:, :]).then_inc(consts_loaded, 16)
            sc.dma_start(spread_sb[:, :, :], spread[:, :, :]).then_inc(spread_loaded, 16)
            sc.wait_ge(consts_loaded, 16)
            for h in range(H):
                sc.wait_ge(wb_made, 2 * h + 2)
                nc.scalar.activation(wb[:, h, :, 1], wb_ps[2 * (h % 2) + 1][:, 0:DUOS], ACT.Identity,
                                     bias=w1_goods[:, h:h + 1]).then_inc(wb_kept[1], 1)
            sc.wait_ge(bias_kept, 2)

            def keep(k, bank, made=BLOCK):
                sc.wait_ge(w_made, BLOCK * k + made)
                if not isinstance(k, int) or k >= 1:
                    for m in range(COL_TILES):
                        sc.wait_ge(stack_loaded[m], 16 * k)
                nc.scalar.activation(wsum[:, bank, :], w_ps[bank][:, 0:N], ACT.Identity, bias=b2).then_inc(w_kept, 1)
                nc.scalar.activation(parts[:, 0, :], w_ps[bank][:, 0:N], ACT.Identity, bias=b2).then_inc(w_kept, 1)

            def step(turn, u):
                tile = SLOTS * turn + u
                if u % 4 == 0 and reached(turn, u, ACT_SLOTS):
                    sc.wait_ge(w_made, tile + 4 - ACT_SLOTS)
                for half in range(2):
                    sc.wait_ge(z_done, 2 * tile + half + 1)
                    for a in range(2):
                        last = nc.scalar.activation(act[0:ROWS, u % ACT_SLOTS, 2 * half + a, :],
                                                    z_ps[u % 2][half][0:ROWS, N * a:N * a + N], ACT.Sigmoid,
                                                    bias=bias_flat[0:ROWS, bass.ds(U * tile + 2 * half + a, 1)])
                    last.then_inc(act_done, 1)
                first = u + 1 - CUT_AT
                if first % BLOCK == 0 and reached(turn, u, CUT_AT - 1):
                    keep(TURN_BLOCKS * turn + first // BLOCK, first // BLOCK % 2)

            turns(sc, step)
            for u in range(REST):
                step(TURNS, u)
            keep(BLOCKS, 0, REST + 1)

        @block.vector
        def _(dve):
            dve.wait_ge(consts_loaded, 16)
            for h in range(H):
                dve.wait_ge(wb_made, 2 * h + 1)
                nc.vector.tensor_scalar(wb[:, h, :, 0], wb_ps[2 * (h % 2)][:, 0:DUOS], w1_goods[:, h:h + 1], None,
                                        ALU.add).then_inc(wb_kept[0], 1)
            for a in range(2):
                dve.wait_ge(bias_made, a + 1)
                nc.vector.tensor_scalar(bias[:, :, a], spread_ps[a][:, 0:DUOS], b1[:, a:a + 1], None,
                                        ALU.add).then_inc(bias_kept, 1)

            def cut(k, half):
                dve.wait_ge(w_kept, 2 * k + 2)
                nc.vector.tensor_tensor(left[:, :], wsum[:, half, :], parts[:, 0, :], ALU.subtract).then_inc(part_step, 1)
                dve.wait_ge(part_step, 3 * k + 1)
                nc.vector.tensor_copy(parts[:, 1, :], left[:, :]).then_inc(part_step, 1)
                dve.wait_ge(part_step, 3 * k + 2)
                nc.vector.tensor_tensor(parts[:, 2, :], left[:, :], parts[:, 1, :],
                                        ALU.subtract).then_inc(part_step, 1)

            def visits(turn, v):
                return SLOTS // WIDE_SLOTS * turn + v // WIDE_SLOTS

            def pool_tile(turn, v):
                tile = SLOTS * turn + v
                if v % STORE == 0 and (not isinstance(tile, int) or tile >= SLOTS):
                    dve.wait_ge(out_stored[v // STORE % 2], 16 * (turn + v // SLOTS))
                for half in range(2):
                    if half == 0:
                        dve.wait_ge(wide_loaded[v % WIDE_SLOTS], 16 * (WIDE * (visits(turn, v)) + WIDE))
                    dve.wait_ge(spread_done, 2 * tile + half + 1)
                    for a in range(2):
                        unit = 2 * half + a
                        column = v % SLOTS * U + unit
                        if half < WIDE and a == 0:
                            sums = wide[:, v % WIDE_SLOTS, half, :]
                        else:
                            sums = spread_ps[half][:, N * a:N * a + N]
                        last = nc.vector.tensor_tensor_reduce(
                            goods[:, v % SLOTS, unit, :], sums, goods[:, v % SLOTS, unit, :],
                            1.0, 0.0, ALU.mult, ALU.add, out_stage[:, column:column + 1])
                    last.then_inc(pooled, 1)

            def step(turn, u):
                if reached(turn, u, LAG):
                    pool_tile(turn, u - LAG)
                first = u - CUT_AT
                if first % BLOCK == 0 and reached(turn, u, CUT_AT):
                    cut(TURN_BLOCKS * turn + first // BLOCK, first // BLOCK % 2)

            turns(dve, step)
            for u in range(LAG + REST):
                pool_tile(TURNS, u - LAG)
                if u == CUT_AT - BLOCK:
                    cut(BLOCKS - 1, 1)
                if u == CUT_AT - 1:
                    cut(BLOCKS, 0)


def kernel(r_goods, r_candidate_ad, L0_rec_W1, L0_rec_b1, L0_rec_W2, L0_rec_b2):
    import numpy as np
    import concourse.bacc as bacc
    from concourse.bass_utils import run_bass_kernel_spmd

    f32 = np.float32
    w1 = np.asarray(L0_rec_W1)
    b1 = np.asarray(L0_rec_b1)
    w2 = np.asarray(L0_rec_W2)[:, 0]
    w1_cand, w1_goods, w1_out = w1[:K], w1[K:2 * K], w1[2 * K:].reshape(K, K, H)

    batch_of = np.array([[DUO_B * d + (q if a == 0 else 4 + q if q < 3 else 3) for q in range(Q)]
                         for d in range(DUOS) for a in range(2)])
    goods = np.zeros((DUO_B * DUOS, N, K), f32)
    goods[:B] = np.asarray(r_goods)
    cands = np.zeros((DUO_B * DUOS, K), f32)
    cands[:B] = np.asarray(r_candidate_ad)
    goods_t = np.ascontiguousarray(goods[batch_of].transpose(1, 3, 0, 2)).reshape(P, TILES, U * N)
    cand_t = np.ascontiguousarray(
        cands[batch_of].reshape(DUOS, 2, Q, K).transpose(2, 3, 1, 0)).reshape(P, 2, DUOS)

    w1_outer = np.zeros((Q, K, H, Q, K), f32)
    w1a = np.zeros((Q, K, 2, P), f32)
    b1c = np.zeros((P, 2), f32)
    w2c = np.zeros((P, DUOS_C, 2, 32), f32)
    qmask = np.zeros((Q, K, Q), f32)
    spread = np.zeros((32, PARTS, DUOS_C, 2, Q, K), mybir.dt.np(BF16))
    for q in range(Q):
        w1_outer[q, :, :, q, :] = w1_out.transpose(0, 2, 1)
        qmask[q, :, q] = 1.0
        for a in range(2):
            hs = slice(0, H) if q < 3 else slice(HALF_H * a, HALF_H * (a + 1))
            rows = slice(H * q, H * q + H) if q < 3 else slice(3 * H, ROWS)
            w1a[q, :, a, rows] = w1_cand[:, hs]
            b1c[rows, a] = b1[hs]
            for d in range(DUOS_C):
                batch = DUO_B * d + batch_of[a, q]
                w2c[rows, d, a, batch] = w2[hs]
                spread[batch, :, d, a, q, :] = 1.0
    small = np.zeros((P, C_ALL), f32)
    small[:, C_QMASK:C_B1] = qmask.reshape(P, Q)
    small[:, C_B1:C_B2] = b1c
    small[:, C_B2] = np.asarray(L0_rec_b2)[0]
    small[:, C_W1B:C_W1A] = np.tile(w1_goods, (Q, 1))
    small[:, C_W1A:C_W2] = w1a.reshape(P, 2 * P)
    small[:, C_W2:C_ALL] = w2c.reshape(P, DUOS_C * 2 * 32)

    nc = bacc.Bacc("TRN2", target_bir_lowering=False, num_devices=1)
    arrays, args = {}, []
    for name, a in (("goods_t", goods_t), ("cand_t", cand_t), ("w1_outer", w1_outer.reshape(P, H, P)),
                    ("small", small), ("spread", spread.reshape(PARTS * 32, DUOS_C * 2, P))):
        arrays[name] = a
        args.append(nc.dram_tensor(name, a.shape, mybir.dt.from_np(a.dtype), kind="ExternalInput").ap())
    out_t = nc.dram_tensor("out_t", (P, UNITS), F32, kind="ExternalOutput").ap()
    build(nc, *args, out_t)
    r = run_bass_kernel_spmd(nc, [arrays], core_ids=[0])
    got = np.asarray(r.results[0]["out_t"]).reshape(Q, K, DUOS, 2).transpose(2, 3, 0, 1)
    batches = np.concatenate((got[:, 0], got[:, 1, 0:3]), axis=1)
    return np.ascontiguousarray(batches.reshape(DUO_B * DUOS, K)[:B])
```

```python
from contextlib import ExitStack

import concourse.bass as bass
from concourse import mybir

F32 = mybir.dt.float32
BF16 = mybir.dt.bfloat16
ALU = mybir.AluOpType
ACT = mybir.ActivationFunctionType

P = 128
B, N, K, H = 2048, 200, 32, 36
Q = 4
HALF_H = H // 2
ROWS = 3 * H + HALF_H
DUO_B = 7
U = 4
DUOS = 294
UNITS = 2 * DUOS
TILES = UNITS // U
BLOCK = 4
COL_TILES = 4
DUOS_C = BLOCK * U // 2 // COL_TILES
SLOTS = 16
TURNS = TILES // SLOTS
REST = TILES - TURNS * SLOTS
TURN_BLOCKS = SLOTS // BLOCK
BLOCKS = TURNS * TURN_BLOCKS
ACT_SLOTS = 8
BD_SLOTS = 4
TAIL = TURNS * SLOTS - BLOCK
SUM_LAG = 2
LAG = 10
PARTS = 3
CUT_AT = BLOCK + 2
WIDEN_AT = (11, 12, 13, 14)
BY_DMA = (2, 1)
WIDE_SLOTS = 2 * BLOCK
LOAD = 2
STORE = 8
W1_CHUNKS = 6
BANK = 512

C_QMASK = 0
C_SHORT = C_QMASK + 3 * U
C_B1 = C_SHORT + 2
C_B2 = C_B1 + 2
C_W1B = C_B2 + 1
C_W1A = C_W1B + H
C_W2 = C_W1A + 2 * P
C_ALL = C_W2 + DUOS_C * 2 * 32


def build(nc, goods_t, cand_t, w1_outer, small, spread, out_t):
    with ExitStack() as ctx:
        def sb(name, shape, dt=F32):
            return ctx.enter_context(nc.sbuf_tensor(name, shape, dt))

        def ps(name, shape):
            return ctx.enter_context(nc.psum_tensor(name, shape, F32))

        def sem(name):
            return ctx.enter_context(nc.semaphore(name))

        goods = sb("goods", [P, SLOTS, U, N])
        act = sb("act", [P, ACT_SLOTS, U, N])
        wb = sb("wb", [P, H, DUOS, 2])
        bd = sb("bd", [P, BD_SLOTS, U, ROWS])
        consts = sb("consts", [P, C_ALL])
        spread_sb = sb("spread_sb", [PARTS * 32, DUOS_C * 2, P], BF16)
        bias = sb("bias", [P, DUOS, 2])
        wsum = sb("wsum", [P, TURN_BLOCKS, N])
        wide = sb("wide", [P, WIDE_SLOTS, 2, N])
        left = sb("left", [P, N])
        parts = sb("parts", [P, 2, PARTS, N], BF16)
        stack = sb("stack", [PARTS * 32, 2, COL_TILES, N], BF16)
        out_stage = sb("out_stage", [P, SLOTS * U])

        act_flat = act[:, :, :, :].rearrange("p t u n -> p (t u n)")
        w1_bd = act_flat[:, 0:H * P].rearrange("p (h c) -> p h c", h=H)
        cand = act_flat[:, H * P:H * P + UNITS].rearrange("p (a d) -> p a d", a=2)

        qmask = consts[:, C_QMASK:C_SHORT].rearrange("p (u b) -> p u b", b=3)
        short_mask = consts[:, C_SHORT:C_B1]
        b1 = consts[:, C_B1:C_B1 + 2]
        b2 = consts[:, C_B2:C_B2 + 1]
        w1_goods = consts[:, C_W1B:C_W1B + H]
        w1_cand = consts[:, C_W1A:C_W1A + 2 * P].rearrange("p (a c) -> p a c", a=2)
        w2 = consts[:, C_W2:C_ALL].rearrange("p (v c) -> p v c", c=32)
        bias_flat = bias[:, :, :].rearrange("p d a -> p (d a)")

        z_ps = [[ps(f"z_ps{a}{b}", [P, BANK]) for b in range(2)] for a in range(2)]
        w_ps = [ps(f"w_ps{a}", [P, BANK]) for a in range(2)]
        spread_ps = [ps(f"spread_ps{a}", [P, BANK]) for a in range(2)]
        wb_ps = [z_ps[0][0], z_ps[0][1], z_ps[1][0], z_ps[1][1]]

        consts_loaded = sem("consts_loaded")
        cand_loaded = sem("cand_loaded")
        spread_loaded = sem("spread_loaded")
        w1_loaded = [sem(f"w1_loaded{i}") for i in range(W1_CHUNKS)]
        goods_loaded = [sem(f"goods_loaded{i}") for i in range(SLOTS // LOAD)]
        stack_loaded = [[sem(f"stack_loaded{i}{m}") for m in range(COL_TILES)] for i in range(2)]
        wide_loaded = [sem(f"wide_loaded{i}") for i in range(WIDE_SLOTS)]
        out_stored = [sem(f"out_stored{i}") for i in range(SLOTS // STORE)]
        wb_made = sem("wb_made")
        wb_kept = [sem("wb_kept0"), sem("wb_kept1")]
        bias_made = sem("bias_made")
        bias_kept = sem("bias_kept")
        bd_ready = sem("bd_ready")
        z_done = sem("z_done")
        act_done = sem("act_done")
        w_made = sem("w_made")
        w_kept = sem("w_kept")
        part_step = sem("part_step")
        spread_done = sem("spread_done")
        pooled = sem("pooled")

        block = ctx.enter_context(nc.Block())

        def turns(eng, step):
            for u in range(SLOTS):
                step(0, u)
            with eng.Fori(1, TURNS) as turn:
                for u in range(SLOTS):
                    step(turn, u)

        def reached(turn, u, least):
            return not isinstance(turn, int) or SLOTS * turn + u >= least

        def moved(turn, b):
            return 16 * (TURN_BLOCKS // 2 * turn + b // 2 + 1)

        def at_end(turn, v):
            return isinstance(turn, int) and SLOTS * turn + v >= TAIL

        def by_dma(turn, v):
            return 0 if at_end(turn, v) else BY_DMA[v % 2]

        def spreads(turn, v, half):
            if at_end(turn, v):
                return 3 * TAIL // 2 + 2 * (SLOTS * turn + v - TAIL) + half + 1
            return 3 * SLOTS // 2 * turn + 3 * (v // 2) + 2 * (v % 2) + half

        @block.sync
        def _(sp):
            sp.dma_start(cand, cand_t[:, :, :]).then_inc(cand_loaded, 16)
            step_h = H // W1_CHUNKS
            for c in range(W1_CHUNKS):
                sp.dma_start(w1_bd[:, c * step_h:(c + 1) * step_h, :],
                             w1_outer[:, c * step_h:(c + 1) * step_h, :]).then_inc(w1_loaded[c], 16)

            def move(turn, b):
                sp.wait_ge(part_step, 3 * (TURN_BLOCKS * turn + b) + 3)
                if isinstance(turn, int) and turn == TURNS and b == 0:
                    sp.wait_ge(spread_done, spreads(TURNS, -1 - BLOCK, 1))
                for m in range(0 if at_end(turn, BLOCK * b) else 1, COL_TILES):
                    sp.dma_start(stack[:, b % 2, m, :],
                                 parts[32 * m:32 * m + 32, b % 2, :, :]).then_inc(stack_loaded[b % 2][m], 16)

            def widen(b, v, units):
                slot = BLOCK * (b % 2) + v
                for w in range(units):
                    row = 32 * (v % 2 * 2) + DUO_B * (v // 2) + 3 * w
                    sp.dma_start(wide[:, slot, w, :],
                                 wsum[row:row + Q, b % TURN_BLOCKS, :].unsqueeze(1).broadcast_to([Q, K, N])
                                 ).then_inc(wide_loaded[slot], 16)

            def moves(turn, u):
                for v, at in enumerate(WIDEN_AT):
                    first = u - at
                    if first % BLOCK == 0 and reached(turn, u, at):
                        b = first // BLOCK
                        if v == 0 and not at_end(turn, first):
                            sp.wait_ge(w_kept, 2 * (TURN_BLOCKS * turn + b) + 2)
                        if v == 1:
                            move(turn, b)
                        widen(b, v, by_dma(turn, first + v))

            def store(turn, offset, tiles):
                tile = SLOTS * turn + offset
                sp.wait_ge(pooled, 2 * (tile + tiles))
                sp.dma_start(out_t[:, bass.ds(U * tile, U * tiles)],
                             out_stage[:, U * offset:U * (offset + tiles)]).then_inc(out_stored[offset // STORE], 16)

            def step(turn, u):
                moves(turn, u)
                if u % STORE == STORE - 1 and reached(turn, u, SLOTS):
                    store(turn - 1, u + 1 - STORE, STORE)
                if u % LOAD == 0:
                    load(turn, u, LOAD)

            def load(turn, u, tiles):
                tile = SLOTS * turn + u
                if reached(turn, u, SLOTS):
                    sp.wait_ge(pooled, 2 * (tile - SLOTS + tiles))
                sp.dma_start(goods[:, u:u + tiles, :, :].rearrange("p t s n -> p (t s n)"),
                             goods_t[:, bass.ds(tile, tiles), :].rearrange("p t n -> p (t n)")
                             ).then_inc(goods_loaded[u // LOAD], 16)

            turns(sp, step)
            for u in range(WIDEN_AT[1] + 1):
                if u < REST and u % LOAD == 0:
                    load(TURNS, u, min(LOAD, REST - u))
                moves(TURNS, u)
            store(TURNS - 1, 0, STORE)
            store(TURNS - 1, STORE, STORE)
            store(TURNS, 0, REST)
            sp.wait_ge(out_stored[0], 16 * (TURNS + 1))
            sp.wait_ge(out_stored[1], 16 * TURNS)

        @block.gpsimd
        def _(pool):
            pool.wait_ge(consts_loaded, 16)
            pool.wait_ge(wb_kept[0], H)
            pool.wait_ge(wb_kept[1], H)

            def step(turn, u):
                slot = u % BD_SLOTS
                tile = SLOTS * turn + u
                if reached(turn, u, BD_SLOTS):
                    pool.wait_ge(z_done, 2 * (tile - BD_SLOTS) + 2)
                src = wb[:, :, bass.ds(U // 2 * tile, U // 2), :].rearrange("p h d a -> p (d a) h")
                nc.gpsimd.tensor_tensor(
                    bd[:, slot, :, 0:3 * H].rearrange("p u (b h) -> p u b h", b=3),
                    src.unsqueeze(2).broadcast_to([P, U, 3, H]),
                    qmask.unsqueeze(3).broadcast_to([P, U, 3, H]), ALU.mult).then_inc(bd_ready, 1)
                for a in range(2):
                    src = wb[:, HALF_H * a:HALF_H * (a + 1), bass.ds(U // 2 * tile, U // 2), a]
                    nc.gpsimd.tensor_tensor(
                        bd[:, slot, a::2, 3 * H:ROWS], src.rearrange("p h d -> p d h"),
                        short_mask[:, a:a + 1].unsqueeze(1).broadcast_to([P, U // 2, HALF_H]),
                        ALU.mult).then_inc(bd_ready, 1)

            turns(pool, step)
            for u in range(REST):
                step(TURNS, u)

        @block.tensor
        def _(pe):
            pe.wait_ge(cand_loaded, 16)
            for h in range(H):
                if h % (H // W1_CHUNKS) == 0:
                    pe.wait_ge(w1_loaded[h // (H // W1_CHUNKS)], 16)
                for a in range(2):
                    if h >= 2:
                        pe.wait_ge(wb_kept[a], h - 1)
                    nc.tensor.matmul(wb_ps[2 * (h % 2) + a][:, 0:DUOS], w1_bd[:, h, :], cand[:, a, :],
                                     start=True, stop=True).then_inc(wb_made, 1)
            pe.wait_ge(consts_loaded, 16)
            for a in range(2):
                nc.tensor.matmul(spread_ps[a][:, 0:DUOS], w1_cand[:, a, :], cand[:, a, :],
                                 start=True, stop=True).then_inc(bias_made, 1)
            pe.wait_ge(spread_loaded, 16)
            pe.wait_ge(bias_kept, 2)

            def row_sums(turn, v, a, tiles=2):
                tile = SLOTS * turn + v
                k = TURN_BLOCKS * turn + v // BLOCK
                if a == 0:
                    pe.wait_ge(act_done, 2 * (tile + tiles))
                    if v % BLOCK == 0 and (not isinstance(k, int) or k >= 2):
                        pe.wait_ge(w_kept, 2 * (k - 1))
                d = v % BLOCK // 2
                short = isinstance(tile, int) and tile + 2 > TILES
                for m in range(U // 2 * tiles):
                    last = nc.tensor.matmul(w_ps[v // BLOCK % 2][32 * m:32 * m + 32, 0:N], w2[0:ROWS, 2 * d + a, :],
                                            act[0:ROWS, (v + m // 2) % ACT_SLOTS, m % 2 * 2 + a, :],
                                            start=(d == 0 and a == 0),
                                            stop=(a == 1 and (d == DUOS_C - 1 or isinstance(tile, int)
                                                              and tile + 2 * tiles > TILES)),
                                            skip_group_check=True)
                last.then_inc(w_made, 1)

            def spread_half(turn, v, half):
                tile = SLOTS * turn + v
                m, d = v % 2 * 2 + half, v % BLOCK // 2
                first = by_dma(turn, v) if half == 0 else 0
                if first == 2:
                    return
                if v % BLOCK < 2:
                    pe.wait_ge(stack_loaded[v // BLOCK % 2][m], 16 if m == 0 else moved(turn, v // BLOCK))
                if not isinstance(tile, int) or tile >= 1:
                    pe.wait_ge(pooled, 2 * (tile - 1) + half + 1)
                for a in range(first, 2):
                    last = nc.tensor.matmul(spread_ps[half][:, N * a:N * a + N], spread_sb[:, 2 * d + a, :],
                                            stack[:, (v // BLOCK) % 2, m, :], start=True, stop=True)
                last.then_inc(spread_done, 1)

            def products(turn, u, half):
                tile = SLOTS * turn + u
                if half == 0:
                    if u % LOAD == 0:
                        pe.wait_ge(goods_loaded[u // LOAD], 16 * (turn + 1))
                    pe.wait_ge(bd_ready, 3 * tile + 3)
                if reached(turn, u, 2):
                    pe.wait_ge(act_done, 2 * (tile - 2) + half + 1)
                for a in range(2):
                    last = nc.tensor.matmul(z_ps[u % 2][half][0:ROWS, N * a:N * a + N],
                                            bd[:, u % BD_SLOTS, 2 * half + a, :], goods[:, u, 2 * half + a, :],
                                            start=True, stop=True)
                last.then_inc(z_done, 1)

            def step(turn, u):
                for half in range(2):
                    if reached(turn, u, LAG):
                        if u % 2 == 1:
                            spread_half(turn, u - LAG, half)
                        elif half == 0:
                            spread_half(turn, u - LAG, 1)
                    products(turn, u, half)
                if reached(turn, u, SUM_LAG):
                    row_sums(turn, u - 2 - u % 2, u % 2)

            turns(pe, step)
            for u in range(REST):
                step(TURNS, u)
            row_sums(TURNS, 0, 1)
            for a in range(2):
                row_sums(TURNS, 2, a, tiles=1)
            for u in range(REST, LAG + REST):
                for half in range(2):
                    spread_half(TURNS, u - LAG, half)

        @block.scalar
        def _(sc):
            sc.dma_start(consts[:, :], small[:, :]).then_inc(consts_loaded, 16)
            sc.dma_start(spread_sb[:, :, :], spread[:, :, :]).then_inc(spread_loaded, 16)
            sc.wait_ge(consts_loaded, 16)
            for h in range(H):
                sc.wait_ge(wb_made, 2 * h + 2)
                nc.scalar.activation(wb[:, h, :, 1], wb_ps[2 * (h % 2) + 1][:, 0:DUOS], ACT.Identity,
                                     bias=w1_goods[:, h:h + 1]).then_inc(wb_kept[1], 1)
            sc.wait_ge(bias_kept, 2)

            def keep(turn, b, made=BLOCK):
                sc.wait_ge(w_made, BLOCK * (TURN_BLOCKS * turn + b) + made)
                if not isinstance(turn, int) or TURN_BLOCKS * turn + b >= 2:
                    for m in range(1, COL_TILES):
                        sc.wait_ge(stack_loaded[b % 2][m], moved(turn, b - 2))
                for kept in (wsum[:, b % TURN_BLOCKS, :], parts[:, b % 2, 0, :]):
                    nc.scalar.activation(kept, w_ps[b % 2][:, 0:N], ACT.Identity, bias=b2).then_inc(w_kept, 1)

            def step(turn, u):
                tile = SLOTS * turn + u
                if u % 4 == 0 and reached(turn, u, ACT_SLOTS):
                    sc.wait_ge(w_made, tile + 4 - ACT_SLOTS)
                for half in range(2):
                    sc.wait_ge(z_done, 2 * tile + half + 1)
                    for a in range(2):
                        last = nc.scalar.activation(act[0:ROWS, u % ACT_SLOTS, 2 * half + a, :],
                                                    z_ps[u % 2][half][0:ROWS, N * a:N * a + N], ACT.Sigmoid,
                                                    bias=bias_flat[0:ROWS, bass.ds(U * tile + 2 * half + a, 1)])
                    last.then_inc(act_done, 1)
                first = u + 1 - CUT_AT
                if first % BLOCK == 0 and reached(turn, u, CUT_AT - 1):
                    keep(turn, first // BLOCK)

            turns(sc, step)
            for u in range(REST):
                step(TURNS, u)
            keep(TURNS, 0, REST + 1)

        @block.vector
        def _(dve):
            dve.wait_ge(consts_loaded, 16)
            for h in range(H):
                dve.wait_ge(wb_made, 2 * h + 1)
                nc.vector.tensor_scalar(wb[:, h, :, 0], wb_ps[2 * (h % 2)][:, 0:DUOS], w1_goods[:, h:h + 1], None,
                                        ALU.add).then_inc(wb_kept[0], 1)
            for a in range(2):
                dve.wait_ge(bias_made, a + 1)
                nc.vector.tensor_scalar(bias[:, :, a], spread_ps[a][:, 0:DUOS], b1[:, a:a + 1], None,
                                        ALU.add).then_inc(bias_kept, 1)

            def cut(turn, b):
                k, half = TURN_BLOCKS * turn + b, b % 2
                dve.wait_ge(w_kept, 2 * k + 2)
                nc.vector.tensor_tensor(left[:, :], wsum[:, b % TURN_BLOCKS, :], parts[:, half, 0, :], ALU.subtract).then_inc(part_step, 1)
                dve.wait_ge(part_step, 3 * k + 1)
                nc.vector.tensor_copy(parts[:, half, 1, :], left[:, :]).then_inc(part_step, 1)
                dve.wait_ge(part_step, 3 * k + 2)
                nc.vector.tensor_tensor(parts[:, half, 2, :], left[:, :], parts[:, half, 1, :],
                                        ALU.subtract).then_inc(part_step, 1)

            def visits(turn, v):
                return SLOTS // WIDE_SLOTS * turn + v // WIDE_SLOTS

            def pool_tile(turn, v):
                tile = SLOTS * turn + v
                if v % STORE == 0 and (not isinstance(tile, int) or tile >= SLOTS):
                    dve.wait_ge(out_stored[v // STORE % 2], 16 * (turn + v // SLOTS))
                for half in range(2):
                    units = by_dma(turn, v) if half == 0 else 0
                    if units:
                        dve.wait_ge(wide_loaded[v % WIDE_SLOTS], 16 * units * (visits(turn, v) + 1))
                    if units < 2:
                        dve.wait_ge(spread_done, spreads(turn, v, half))
                    for a in range(2):
                        unit = 2 * half + a
                        column = v % SLOTS * U + unit
                        if a < units:
                            sums = wide[:, v % WIDE_SLOTS, a, :]
                        else:
                            sums = spread_ps[half][:, N * a:N * a + N]
                        last = nc.vector.tensor_tensor_reduce(
                            goods[:, v % SLOTS, unit, :], sums, goods[:, v % SLOTS, unit, :],
                            1.0, 0.0, ALU.mult, ALU.add, out_stage[:, column:column + 1])
                    last.then_inc(pooled, 1)

            def step(turn, u):
                if reached(turn, u, LAG):
                    pool_tile(turn, u - LAG)
                first = u - CUT_AT
                if first % BLOCK == 0 and reached(turn, u, CUT_AT):
                    cut(turn, first // BLOCK)

            turns(dve, step)
            for u in range(LAG + REST):
                pool_tile(TURNS, u - LAG)
                if u == CUT_AT - BLOCK:
                    cut(TURNS, -1)
                if u == REST + 1:
                    cut(TURNS, 0)


def kernel(r_goods, r_candidate_ad, L0_rec_W1, L0_rec_b1, L0_rec_W2, L0_rec_b2):
    import numpy as np
    import concourse.bacc as bacc
    from concourse.bass_utils import run_bass_kernel_spmd

    f32 = np.float32
    w1 = np.asarray(L0_rec_W1)
    b1 = np.asarray(L0_rec_b1)
    w2 = np.asarray(L0_rec_W2)[:, 0]
    w1_cand, w1_goods, w1_out = w1[:K], w1[K:2 * K], w1[2 * K:].reshape(K, K, H)

    batch_of = np.array([[DUO_B * d + q + 3 * a for q in range(Q)]
                         for d in range(DUOS) for a in range(2)])
    goods = np.zeros((DUO_B * DUOS, N, K), f32)
    goods[:B] = np.asarray(r_goods)
    cands = np.zeros((DUO_B * DUOS, K), f32)
    cands[:B] = np.asarray(r_candidate_ad)
    goods_t = np.ascontiguousarray(goods[batch_of].transpose(1, 3, 0, 2)).reshape(P, TILES, U * N)
    cand_t = np.ascontiguousarray(
        cands[batch_of].reshape(DUOS, 2, Q, K).transpose(2, 3, 1, 0)).reshape(P, 2, DUOS)

    w1_outer = np.zeros((Q, K, H, Q, K), f32)
    w1a = np.zeros((Q, K, 2, P), f32)
    b1c = np.zeros((P, 2), f32)
    w2c = np.zeros((P, DUOS_C, 2, 32), f32)
    qmask = np.zeros((Q, K, U // 2, 2, 3), f32)
    short_mask = np.zeros((Q, K, 2), f32)
    spread = np.zeros((32, PARTS, DUOS_C, 2, Q, K), mybir.dt.np(BF16))
    for q in range(Q):
        w1_outer[q, :, :, q, :] = w1_out.transpose(0, 2, 1)
        for a in range(2):
            whole = q - a
            if q + 3 * a == 3:
                hs, rows = slice(HALF_H * a, HALF_H * (a + 1)), slice(3 * H, ROWS)
                short_mask[q, :, a] = 1.0
            else:
                hs, rows = slice(0, H), slice(H * whole, H * whole + H)
                qmask[q, :, :, a, whole] = 1.0
            w1a[q, :, a, rows] = w1_cand[:, hs]
            b1c[rows, a] = b1[hs]
            for d in range(DUOS_C):
                batch = DUO_B * d + batch_of[a, q]
                w2c[rows, d, a, batch] = w2[hs]
                spread[batch, :, d, a, q, :] = 1.0
    small = np.zeros((P, C_ALL), f32)
    small[:, C_QMASK:C_SHORT] = qmask.reshape(P, 3 * U)
    small[:, C_SHORT:C_B1] = short_mask.reshape(P, 2)
    small[:, C_B1:C_B2] = b1c
    small[:, C_B2] = np.asarray(L0_rec_b2)[0]
    small[:, C_W1B:C_W1A] = np.tile(w1_goods, (Q, 1))
    small[:, C_W1A:C_W2] = w1a.reshape(P, 2 * P)
    small[:, C_W2:C_ALL] = w2c.reshape(P, DUOS_C * 2 * 32)

    nc = bacc.Bacc("TRN2", target_bir_lowering=False, num_devices=1)
    arrays, args = {}, []
    for name, a in (("goods_t", goods_t), ("cand_t", cand_t), ("w1_outer", w1_outer.reshape(P, H, P)),
                    ("small", small), ("spread", spread.reshape(PARTS * 32, DUOS_C * 2, P))):
        arrays[name] = a
        args.append(nc.dram_tensor(name, a.shape, mybir.dt.from_np(a.dtype), kind="ExternalInput").ap())
    out_t = nc.dram_tensor("out_t", (P, UNITS), F32, kind="ExternalOutput").ap()
    build(nc, *args, out_t)
    r = run_bass_kernel_spmd(nc, [arrays], core_ids=[0])
    got = np.asarray(r.results[0]["out_t"]).reshape(Q, K, DUOS, 2).transpose(2, 3, 0, 1)
    batches = np.concatenate((got[:, 0], got[:, 1, 1:]), axis=1)
    return np.ascontiguousarray(batches.reshape(DUO_B * DUOS, K)[:B])
```
